# Optimizing a Trainium2 kernel written in Bass

```python
import numpy as np
import jax
import jax.numpy as jnp

def _softmax(x, axis=-1):
    return jax.nn.softmax(x, axis=axis)

def _gelu(x):
    return jax.nn.gelu(x, approximate=True)

def _silu(x):
    return jax.nn.silu(x)

def _sigmoid(x):
    return jax.nn.sigmoid(x)

def _layernorm(x, axis=-1, eps=1e-05):
    m = jnp.mean(x, axis=axis, keepdims=True)
    v = jnp.var(x, axis=axis, keepdims=True)
    return (x - m) / jnp.sqrt(v + eps)

def _scatter_add(tgt, idx, src, axis=0):
    return tgt.at[idx].add(src)

def _segment_sum(src, seg, n):
    return jax.ops.segment_sum(src, seg, n)
kernel_name = 'mk_gnn_resnorm_d4_gnn_r16_1344f4'

def setup_inputs(seed: int=0):
    np.random.seed(seed)
    _w = jnp.asarray

    def _rec_inputs():
        import jax
        import jax.numpy as jnp
        _gk = jax.random.key(seed)
        x = -0.000202 + 1 * jax.random.normal(jax.random.fold_in(_gk, 1), (3125, 128), jnp.float32)
        _s = jax.random.randint(jax.random.fold_in(_gk, 2), (25000,), 0, 3125, jnp.int32)
        _d = jax.random.randint(jax.random.fold_in(_gk, 3), (25000,), 0, 3125, jnp.int32)
        _loop = jnp.arange(3125, dtype=jnp.int32)
        src = jnp.concatenate([_s, _d, _loop])
        dst = jnp.concatenate([_d, _s, _loop])
        _o = jnp.argsort(dst, stable=True)
        src = src[_o]
        dst = dst[_o]
        edge_attr_32 = -1.78115e-05 + 1.00007 * jax.random.normal(jax.random.fold_in(_gk, 13), (53125, 32), jnp.float32)
        edge_attr_32_n2 = -1.78115e-05 + 1.00007 * jax.random.normal(jax.random.fold_in(_gk, 14), (53125, 32), jnp.float32)
        edge_type_16 = jax.random.randint(jax.random.fold_in(_gk, 16), (53125,), 0, 16, jnp.int32)
        edge_type_8 = jax.random.randint(jax.random.fold_in(_gk, 17), (53125,), 0, 8, jnp.int32)
        return (x, src, dst, edge_attr_32, edge_attr_32_n2, edge_type_16, edge_type_8)
    x, src, dst, edge_attr_32, edge_attr_32_n2, edge_type_16, edge_type_8 = _rec_inputs()

    def _L0_gnn_setup():
        import jax, jax.numpy as jnp
        import numpy as np
        N_NODES = 3125
        N_EDGES = 37500
        HIDDEN = 128
        N_LAYERS = 4
        key = jax.random.key(seed)
        ks = jax.random.split(key, 6)
        x = jax.random.normal(ks[0], (N_NODES, HIDDEN), dtype=jnp.float32)
        edge_index = jax.random.randint(ks[1], (2, N_EDGES), 0, N_NODES, dtype=jnp.int64)
        batch = jax.random.randint(ks[2], (N_NODES,), 0, 64, dtype=jnp.int64)
        scale = 1.0 / np.sqrt(HIDDEN)
        W1 = jax.random.normal(ks[3], (N_LAYERS, HIDDEN, HIDDEN), dtype=jnp.float32) * scale
        b1 = jnp.zeros((N_LAYERS, HIDDEN), dtype=jnp.float32)
        W2 = jax.random.normal(ks[4], (N_LAYERS, HIDDEN, HIDDEN), dtype=jnp.float32) * scale
        b2 = jnp.zeros((N_LAYERS, HIDDEN), dtype=jnp.float32)
        return {'x': x, 'edge_index': edge_index, 'batch': batch, 'W1': W1, 'b1': b1, 'W2': W2, 'b2': b2}
    _L0_gnn_all = _L0_gnn_setup()
    _L0_gnn_in = {k: v for k, v in _L0_gnn_all.items() if k in ('W1', 'b1', 'W2', 'b2')}
    del _L0_gnn_all

    def _L1_gnn_setup():
        import jax, jax.numpy as jnp
        import numpy as np
        N_NODES = 6250
        N_EDGES = 37500
        D_IN = 128
        D_HID = 128
        N_REL = 8
        key = jax.random.key(seed)
        k = jax.random.split(key, 6)
        x = jax.random.normal(k[0], (N_NODES, D_IN), dtype=jnp.float32)
        edge_index = jax.random.randint(k[1], (2, N_EDGES), 0, N_NODES, dtype=jnp.int32)
        edge_type = jax.random.randint(k[2], (N_EDGES,), 0, N_REL, dtype=jnp.int32)
        W = jax.random.normal(k[3], (N_REL, D_IN, D_HID), dtype=jnp.float32) * 0.05
        root = jax.random.normal(k[4], (D_IN, D_HID), dtype=jnp.float32) * 0.05
        bias = jnp.zeros((D_HID,), dtype=jnp.float32)
        return {'x': x, 'edge_index': edge_index, 'edge_type': edge_type, 'W': W, 'root': root, 'bias': bias}
    _L1_gnn_all = _L1_gnn_setup()
    _L1_gnn_in = {k: v for k, v in _L1_gnn_all.items() if k in ('W', 'root', 'bias')}
    del _L1_gnn_all

    def _L2_gnn_setup():
        import jax, jax.numpy as jnp
        import numpy as np
        N = 3125
        E = 25000
        D_NODE = 128
        D_EDGE = 32
        D_OUT = 128
        R = 16
        B = 8
        key = jax.random.key(seed)
        ks = jax.random.split(key, 12)
        s = 0.05
        return {'vfts': jax.random.normal(ks[0], (N, D_NODE), dtype=jnp.float32), 'adjs': jax.random.randint(ks[1], (2, E), 0, N, dtype=jnp.int32), 'rels': jax.random.randint(ks[2], (E,), 0, R, dtype=jnp.int32), 'embed_rels': jax.random.normal(ks[3], (E, D_EDGE), dtype=jnp.float32), 'embed_rels_target': jax.random.normal(ks[4], (E, D_EDGE), dtype=jnp.float32), 'weight': jax.random.normal(ks[5], (B, D_NODE, D_OUT), dtype=jnp.float32) * s, 'comp': jax.random.normal(ks[6], (R, B), dtype=jnp.float32) * s, 'attn_w1': jax.random.normal(ks[7], (2 * D_NODE + 2 * D_EDGE, D_OUT), dtype=jnp.float32) * s, 'attn_b1': jnp.zeros((D_OUT,), dtype=jnp.float32), 'attn_w2': jax.random.normal(ks[8], (D_OUT, 1), dtype=jnp.float32) * s, 'attn_b2': jnp.zeros((1,), dtype=jnp.float32), 'update': jax.random.normal(ks[9], (D_NODE, D_OUT), dtype=jnp.float32) * s}
    _L2_gnn_all = _L2_gnn_setup()
    _L2_gnn_in = {k: v for k, v in _L2_gnn_all.items() if k in ('weight', 'comp', 'attn_w1', 'attn_b1', 'attn_w2', 'attn_b2', 'update')}
    del _L2_gnn_all

    def _L3_gnn_setup():
        import jax, jax.numpy as jnp
        import numpy as np
        N_NODES = 3125
        N_EDGES = 37500
        IN_FEAT = 128
        OUT_FEAT = 128
        NUM_RELS = 8
        key = jax.random.key(seed)
        ks = jax.random.split(key, 9)
        return {'h': jax.random.normal(ks[0], (N_NODES, IN_FEAT), dtype=jnp.float32), 'W': jax.random.normal(ks[1], (NUM_RELS, IN_FEAT, OUT_FEAT), dtype=jnp.float32) * 0.05, 'bias_term': jax.random.normal(ks[2], (NUM_RELS, OUT_FEAT), dtype=jnp.float32) * 0.05, 'gate_weight': jax.random.normal(ks[3], (NUM_RELS, OUT_FEAT, 1), dtype=jnp.float32) * 0.05, 'gate_bias': jax.random.normal(ks[4], (NUM_RELS, 1), dtype=jnp.float32) * 0.05, 'loop_weight': jax.random.normal(ks[5], (IN_FEAT, OUT_FEAT), dtype=jnp.float32) * 0.05, 'src': jax.random.randint(ks[6], (N_EDGES,), 0, N_NODES, dtype=jnp.int32), 'dst': jax.random.randint(ks[7], (N_EDGES,), 0, N_NODES, dtype=jnp.int32), 'rel': jax.random.randint(ks[8], (N_EDGES,), 0, NUM_RELS, dtype=jnp.int32)}
    _L3_gnn_all = _L3_gnn_setup()
    _L3_gnn_in = {k: v for k, v in _L3_gnn_all.items() if k in ('W', 'bias_term', 'gate_weight', 'gate_bias', 'loop_weight')}
    del _L3_gnn_all
    return {'x': x, 'src': src, 'dst': dst, 'edge_attr_32': edge_attr_32, 'edge_attr_32_n2': edge_attr_32_n2, 'edge_type_16': edge_type_16, 'edge_type_8': edge_type_8, 'L0_gnn_W1': _L0_gnn_in['W1'], 'L0_gnn_b1': _L0_gnn_in['b1'], 'L0_gnn_W2': _L0_gnn_in['W2'], 'L0_gnn_b2': _L0_gnn_in['b2'], 'L1_gnn_W': _L1_gnn_in['W'], 'L1_gnn_root': _L1_gnn_in['root'], 'L1_gnn_bias': _L1_gnn_in['bias'], 'L2_gnn_weight': _L2_gnn_in['weight'], 'L2_gnn_comp': _L2_gnn_in['comp'], 'L2_gnn_attn_w1': _L2_gnn_in['attn_w1'], 'L2_gnn_attn_b1': _L2_gnn_in['attn_b1'], 'L2_gnn_attn_w2': _L2_gnn_in['attn_w2'], 'L2_gnn_attn_b2': _L2_gnn_in['attn_b2'], 'L2_gnn_update': _L2_gnn_in['update'], 'L3_gnn_W': _L3_gnn_in['W'], 'L3_gnn_bias_term': _L3_gnn_in['bias_term'], 'L3_gnn_gate_weight': _L3_gnn_in['gate_weight'], 'L3_gnn_gate_bias': _L3_gnn_in['gate_bias'], 'L3_gnn_loop_weight': _L3_gnn_in['loop_weight']}

def reference(x, src, dst, edge_attr_32, edge_attr_32_n2, edge_type_16, edge_type_8, L0_gnn_W1, L0_gnn_b1, L0_gnn_W2, L0_gnn_b2, L1_gnn_W, L1_gnn_root, L1_gnn_bias, L2_gnn_weight, L2_gnn_comp, L2_gnn_attn_w1, L2_gnn_attn_b1, L2_gnn_attn_w2, L2_gnn_attn_b2, L2_gnn_update, L3_gnn_W, L3_gnn_bias_term, L3_gnn_gate_weight, L3_gnn_gate_bias, L3_gnn_loop_weight):
    import jax
    import jax.numpy as jnp

    def _L0_gnn_ref(x, edge_index, batch, W1, b1, W2, b2):
        import jax, jax.numpy as jnp
        import numpy as np
        N_NODES = 3125
        N_EDGES = 37500
        HIDDEN = 128
        N_LAYERS = 4
        src = edge_index[0]
        dst = edge_index[1]
        n = x.shape[0]
        for l in range(N_LAYERS):
            agg = jax.ops.segment_sum(x[src], dst, num_segments=n)
            h = x + agg
            h = jnp.maximum(h @ W1[l] + b1[l], 0.0)
            x = h @ W2[l] + b2[l]
        return x

    def _L1_gnn_ref(x, edge_index, edge_type, W, root, bias):
        import jax, jax.numpy as jnp
        import numpy as np
        N_NODES = 6250
        N_EDGES = 37500
        D_IN = 128
        D_HID = 128
        N_REL = 8
        "PyG RGCNConv (aggr='mean', root_weight=True, bias=True) + ReLU.\n\n            out[i] = relu( x[i] @ root + bias\n                           + sum_r mean_{j in N_r(i)} (x[j] @ W[r]) )\n            Dropout is identity in eval mode and omitted.\n            "
        n_nodes = x.shape[0]
        n_rel = W.shape[0]
        src, dst = (edge_index[0], edge_index[1])
        out = x @ root + bias
        for r in range(n_rel):
            hr = x @ W[r]
            mask = edge_type == r
            msg = hr[src] * mask[:, None].astype(x.dtype)
            s = jax.ops.segment_sum(msg, dst, num_segments=n_nodes)
            c = jax.ops.segment_sum(mask.astype(x.dtype), dst, num_segments=n_nodes)
            out = out + s / jnp.maximum(c, 1.0)[:, None]
        return jax.nn.relu(out)

    def _L2_gnn_ref(vfts, adjs, rels, embed_rels, embed_rels_target, weight, comp, attn_w1, attn_b1, attn_w2, attn_b2, update):
        import jax, jax.numpy as jnp
        import numpy as np
        N = 3125
        E = 25000
        D_NODE = 128
        D_EDGE = 32
        D_OUT = 128
        R = 16
        B = 8
        src, dst = (adjs[0], adjs[1])
        erps = jnp.concatenate((vfts[src], vfts[dst], embed_rels, embed_rels_target), axis=1)
        h = jax.nn.relu(erps @ attn_w1 + attn_b1)
        alphas = jax.nn.sigmoid(h @ attn_w2 + attn_b2)
        w_rel = (comp @ weight.reshape(B, D_NODE * D_OUT)).reshape(R, D_NODE, D_OUT)
        srcs_dense = jnp.einsum('nd,rdo->rno', vfts, w_rel)
        srcs = alphas[rels] * srcs_dense[rels, src]
        vrps = jnp.zeros((vfts.shape[0], D_OUT), dtype=vfts.dtype)
        vrps = vrps.at[dst].add(srcs)
        dsts = vfts @ update
        vrps = vrps.at[dst].add(dsts[dst])
        return jax.nn.relu(vrps)

    def _L3_gnn_ref(h, W, bias_term, gate_weight, gate_bias, loop_weight, src, dst, rel):
        import jax, jax.numpy as jnp
        import numpy as np
        N_NODES = 3125
        N_EDGES = 37500
        IN_FEAT = 128
        OUT_FEAT = 128
        NUM_RELS = 8
        n_nodes = h.shape[0]
        loop_message = h @ loop_weight
        xw = jnp.einsum('ni,rio->rno', h, W)
        msg = xw[rel, src] + bias_term[rel]
        gw = gate_weight[..., 0]
        gate = jax.nn.sigmoid(jnp.sum(msg * gw[rel], axis=-1) + gate_bias[rel, 0])
        agg = jax.ops.segment_sum(msg * gate[:, None], dst, num_segments=n_nodes)
        node_repr = agg + loop_message
        return jax.nn.relu(node_repr)
    edge_index = jnp.stack([src, dst])
    batch0 = jnp.zeros((3125,), jnp.int32)
    x = _layernorm(x + _L0_gnn_ref(x, edge_index, batch0, L0_gnn_W1, L0_gnn_b1, L0_gnn_W2, L0_gnn_b2), axis=-1)
    x = _layernorm(x + _L1_gnn_ref(x, edge_index, edge_type_8, L1_gnn_W, L1_gnn_root, L1_gnn_bias), axis=-1)
    x = _layernorm(x + _L2_gnn_ref(x, edge_index, edge_type_16, edge_attr_32, edge_attr_32_n2, L2_gnn_weight, L2_gnn_comp, L2_gnn_attn_w1, L2_gnn_attn_b1, L2_gnn_attn_w2, L2_gnn_attn_b2, L2_gnn_update), axis=-1)
    x = _layernorm(x + _L3_gnn_ref(x, L3_gnn_W, L3_gnn_bias_term, L3_gnn_gate_weight, L3_gnn_gate_bias, L3_gnn_loop_weight, src, dst, edge_type_8), axis=-1)
    return x

_drawn_inputs = setup_inputs


def setup_inputs(seed=0):
    import zlib

    import numpy as np

    out = dict(_drawn_inputs(seed))
    spreads = {'L0_gnn_b1': (0.0, 0.287),
     'L0_gnn_b2': (0.0, 0.1),
     'L1_gnn_bias': (0.0, 0.1),
     'L2_gnn_attn_b1': (0.0, 0.8)}
    factors = {'edge_attr_32': 8.0, 'edge_attr_32_n2': 8.0, 'L2_gnn_attn_w1': 8.0, 'L2_gnn_attn_w2': 8.0}
    for name, (base, spread) in spreads.items():
        noise = np.random.default_rng([zlib.crc32(name.encode()), seed]).standard_normal(out[name].shape)
        drawn = base * np.exp(spread * noise) if base else spread * noise
        out[name] = jnp.asarray(drawn.astype(out[name].dtype))
    for name, factor in factors.items():
        out[name] = (out[name] * factor).astype(out[name].dtype)
    return out
```

```python
import concourse.bass as bass
from concourse import mybir
from contextlib import ExitStack

F32 = mybir.dt.float32
BF16 = mybir.dt.bfloat16
I32 = mybir.dt.int32
ALU = mybir.AluOpType
ACT = mybir.ActivationFunctionType
AXX = mybir.AxisListType.X

P = 128
N = 3125
E = 53125
D = 128
DE = 32
BLOCKS = -(-N // P)
NP = BLOCKS * P
LASTN = N - (BLOCKS - 1) * P
TILES = -(-E // P)
STEPS = TILES + BLOCKS - 1
TQ, TC = 104, 4
LAYERS = 4
F = 16
SMALL = 16
R1, R2, R3, BASES = 8, 16, 8, 8
EPS = 1e-5

G = 4
NB = 5
IT = STEPS // (G * NB)
GROUPS = STEPS // G
KB = 512
CH = -(-NP // KB)
QB = 5
NI = BLOCKS // QB
SLOTS = 3
USES = [len(range(s, QB, SLOTS)) for s in range(SLOTS)]
BANKS = 5
assert TQ * TC == TILES and IT * G * NB == STEPS and NI * QB == BLOCKS
HALF = 2 * DE


def chunk(c):
    return min(KB, NP - c * KB)


def gnn(nc, x, src, dst, ea1, ea2, et16, et8, g0w1, g0b1, g0w2, g0b2, g1w, g1root, g1bias,
        g2w, g2comp, g2aw1, g2ab1, g2aw2, g2ab2, g2upd, g3w, g3bias, g3gw, g3gb, g3loop, out):
    with ExitStack() as ctx:
        ctx.enter_context(nc.allow_non_contiguous_dma(reason="small weights"))

        def sb(name, shape, dt=F32):
            return ctx.enter_context(nc.sbuf_tensor(name, shape, dt))

        def ps(name, shape, dt=F32):
            return ctx.enter_context(nc.psum_tensor(name, shape, dt))

        def sem(name):
            return ctx.enter_context(nc.semaphore(name))

        def dram(name, shape):
            return nc.dram_tensor(name, shape, F32, kind="Internal").ap()

        table0 = dram("table0", (NP, D))
        table1 = dram("table1", (NP * R1, D))
        table2 = dram("table2", (NP * R2, D))
        table3 = dram("table3", (NP * R3, D))

        arena = sb("arena", [P, 14336])
        ids_i = arena[0:TQ, 0:2048].bitcast(I32).rearrange("q (k c p) -> q k c p", k=4, c=TC)
        ids_f = arena[0:TQ, 2048:4096].rearrange("q (k c p) -> q k c p", k=4, c=TC)
        cmp_m = arena[0:TQ, 4096:4096 + TC * STEPS].rearrange("q (c s) -> q c s", c=TC)
        sel_m = arena[0:TQ, 6144:6144 + TC * STEPS].rearrange("q (c s) -> q c s", c=TC)
        hT = arena[:, 0:NP]
        rT = arena[:, NP:2 * NP]
        SW = R2 * D
        stage = arena[:, 0:SLOTS * SW].rearrange("p (s w) -> p s w", s=SLOTS)
        l0w = arena[:, 8192:8192 + LAYERS * (3 * D + 2)].rearrange("p (l w) -> p l w", l=LAYERS)
        step_io, bs_f, ts_f, srcs = (arena[:, 9800 + i * STEPS:9800 + (i + 1) * STEPS] for i in range(4))
        iota_i = arena[:, 9800 + 4 * STEPS:9800 + 5 * STEPS + P + R2 + TC].bitcast(I32)
        basis = arena[:, 13000:13000 + BASES * D].rearrange("p (b f) -> p b f", b=BASES)
        hotT = arena[:, 0:NB * G * P].rearrange("p (q j n) -> p q j n", q=NB, j=G)
        xn = sb("xn", [P, BLOCKS, D])
        un = sb("un", [P, BLOCKS, D])
        xT = sb("xT", [P, NP])
        rest = sb("rest", [P, BLOCKS, D])
        msgs = sb("msgs", [P, NB, G, D])
        wattn = sb("wattn", [P, 3, D])
        feT = sb("feT", [HALF, F])
        fidx = sb("fidx", [F, 2], I32)
        xe = sb("xe", [F, 2, D])
        xeT = sb("xeT", [D, 2 * F])
        hsum = sb("hsum", [F, D])
        hdot = sb("hdot", [F, D])
        logit = sb("logit", [F, 1])
        alpha = sb("alpha", [F, 1])
        alphab = sb("alphab", [F, P])
        alphar = sb("alphar", [P, R2])
        relhot2 = sb("relhot2", [P, G, R2])
        wsum2 = sb("wsum2", [P, G, R2])
        rel16 = sb("rel16", [P, STEPS])
        hot = sb("hot", [P, NB, G, P])
        hotb = sb("hotb", [P, NB, G, P], BF16)
        relhot = sb("relhot", [P, NB, G, R1])
        gidx = sb("gidx", [P, NB, G], I32)
        wsum = sb("wsum", [P, G, R1])
        wedge = sb("wedge", [P, NB, G])
        drel = sb("drel", [P, STEPS])
        rel8 = sb("rel8", [P, STEPS])
        idx0 = sb("idx0", [P, STEPS], I32)
        idx8 = sb("idx8", [P, STEPS], I32)
        idx16 = sb("idx16", [P, STEPS], I32)
        walk_i = sb("walk_i", [1, 4, STEPS], I32)
        node_io = sb("node_io", [P, P])
        rel_io = sb("rel_io", [P, R2])
        tile_io = sb("tile_io", [P, TC])
        tmax = sb("tmax", [P, 4, TC])
        tmax_i = sb("tmax_i", [P, 2, TC], I32)
        ident = sb("ident", [P, P])
        identb = sb("identb", [P, P], BF16)
        ones = sb("ones", [P, P])
        zerob = sb("zerob", [P, KB], BF16)
        l0c = sb("l0c", [P, 3 * D + 2])
        tab = sb("tab", [P, (R2 + 1) * D])
        compb = sb("compb", [P, R2, BASES])
        rows = sb("rows", [P, 3, D])
        b3row = sb("b3row", [P, R3, D])
        gwrow = sb("gwrow", [P, R3, D])
        gbrow = sb("gbrow", [P, R3])
        gcon = sb("gcon", [P, R3])
        b2att = sb("b2att", [P, 1])
        epst = sb("epst", [P, 1])
        cnt = sb("cnt", [P, BLOCKS, R1])
        invc = sb("invc", [P, BLOCKS * R1])
        indeg = sb("indeg", [P, BLOCKS])
        xb = sb("xb", [P, QB, D])
        yb = sb("yb", [P, QB, D])
        xTb = sb("xTb", [P, QB, P])
        bst = sb("bst", [P, QB, 6])
        bag = sb("bag", [P, QB, 2])
        std = sb("std", [P, QB])
        rstd = sb("rstd", [P, QB])
        gate = sb("gate", [P, QB, R3])
        glog = sb("glog", [P, QB, R3])

        acc = ps("acc", [P, 7 * KB])
        misc = ps("misc", [P, KB])
        cps = misc[:, 0:BLOCKS * R1]
        hotT_ps = misc[:, 0:KB // 2].bitcast(BF16).rearrange("p (j n) -> p j n", j=G)
        wps = misc[:, KB // 2:KB // 2 + G * R1].rearrange("p (j r) -> p j r", j=G)

        pads_set = sem("pads_set")
        ids_in = sem("ids_in")
        x_in = sem("x_in")
        l0w_in = sem("l0w_in")
        tab_in = sem("tab_in")
        small_in = sem("small_in")
        iota_set = sem("iota_set")
        setup_dve = sem("setup_dve")
        sel_ready = sem("sel_ready")
        walk_ps = sem("walk_ps")
        walk_set = sem("walk_set")
        table0_set = sem("table0_set")
        group_free = sem("group_free")
        gidx_set = sem("gidx_set")
        msgs_in = [sem(f"msgs_in{q}") for q in range(NB)]
        hot_ready = sem("hot_ready")
        relhot_ready = sem("relhot_ready")
        hotb_ready = sem("hotb_ready")
        hotT_ps_full = sem("hotT_ps_full")
        hotT_ready = sem("hotT_ready")
        w_ps_full = sem("w_ps_full")
        w_read = sem("w_read")
        h_ps_full = sem("h_ps_full")
        logit_ready = sem("logit_ready")
        alpha_ready = sem("alpha_ready")
        chain = sem("chain")
        l0c_set = sem("l0c_set")
        hT_ready = sem("hT_ready")
        m1_ps = sem("m1_ps")
        rT_ready = sem("rT_ready")
        xT_ps = sem("xT_ps")
        xT_ready = sem("xT_ready")
        un_ps = sem("un_ps")
        un_ready = sem("un_ready")
        tab_set = sem("tab_set")
        xb_ready = sem("xb_ready")
        bag_ready = sem("bag_ready")
        std_ready = sem("std_ready")
        tp_full = sem("tp_full")
        xTb_ready = sem("xTb_ready")
        bank_full = [sem(f"bank_full{i}") for i in range(BANKS)]
        bank_free = [sem(f"bank_free{i}") for i in range(BANKS)]
        xn_ready = sem("xn_ready")
        glog_ready = sem("glog_ready")
        gate_ready = sem("gate_ready")
        stage_ready = [sem(f"stage_ready{i}") for i in range(SLOTS)]
        stage_out = [sem(f"stage_out{i}") for i in range(SLOTS)]
        xe_in = sem("xe_in")
        xeT_ps = sem("xeT_ps")
        xeT_ready = sem("xeT_ready")
        out_done = sem("out_done")
        block = ctx.enter_context(nc.Block())

        def after(eng, s, value):
            if not (isinstance(value, int) and value <= 0):
                eng.wait_ge(s, value)

        def hold(eng, s, value):
            eng.wait_ge(s, value)
            eng.nop(nofuse=True)

        JOBS = {1: 3, 2: 5, 3: 3}
        PARTS = {1: 0, 2: 0, 3: 1}
        ROW_JOBS = {1: (0, 1), 2: (0, 1, 2, 3), 3: ()}

        def bank_of(ph, q, j):
            return (q * JOBS[ph] + j) % BANKS

        def bank_use(ph, i, q, j):
            return i * JOBS[ph] + (NI * sum(JOBS[p] for p in range(1, ph)) + (q * JOBS[ph] + j) // BANKS)

        def slot_use(ph, i, q):
            return i * USES[q % SLOTS] + ((ph - 1) * NI * USES[q % SLOTS] + q // SLOTS)

        def slot_parts(ph, i, q):
            u = USES[q % SLOTS]
            return i * (u * PARTS[ph]) + (NI * u * sum(PARTS[p] for p in range(1, ph)) + (q // SLOTS + 1) * PARTS[ph])

        def nodes(eng, ph, body):
            if ph == 1:
                body(0)
            with eng.Fori(1 if ph == 1 else 0, NI) as i:
                body(i)

        def seen(ph, i, q=0):
            return i * QB + ((ph - 1) * BLOCKS + q)

        tabw = {1: (R1 + 1) * D, 2: (R2 + 1) * D, 3: (R3 + 1) * D + R3}

        def products(ph):
            if ph == 3:
                return [(R3 * D, (R3 + 1) * D + R3), (0, KB), (KB, 2 * KB)]
            return [(c, min(c + KB, tabw[ph])) for c in range(0, tabw[ph], KB)]

        @block.sync
        def _(sp):
            sp.wait_ge(pads_set, 4)
            full = (E // P) - (TC - 1) * TQ
            for k, a in enumerate((dst, src, et8, et16)):
                sp.dma_start(ids_i[:, k, 0:TC - 1, :],
                             a[0:(TC - 1) * TQ * P].rearrange("(c q p) -> q c p", c=TC - 1, q=TQ)).then_inc(ids_in, 16)
                sp.dma_start(ids_i[0:full, k, TC - 1, :],
                             a[(TC - 1) * TQ * P:(E // P) * P].rearrange("(q p) -> q p", p=P)).then_inc(ids_in, 16)
                sp.dma_start(ids_i[full:full + 1, k, TC - 1, 0:E % P],
                             a[(E // P) * P:E].rearrange("(q p) -> q p", q=1)).then_inc(ids_in, 16)
            sp.dma_start(xn[:, 0:BLOCKS - 1, :],
                         x[0:(BLOCKS - 1) * P].rearrange("(b p) f -> p b f", p=P)).then_inc(x_in, 16)
            sp.dma_start(xn[0:LASTN, BLOCKS - 1, :], x[(BLOCKS - 1) * P:N]).then_inc(x_in, 16)
            sp.dma_start(table0[0:N], x).then_inc(table0_set, 16)
            sp.dma_start(table0[N:NP], xn[LASTN:P, BLOCKS - 1, :]).then_inc(table0_set, 16)
            for l in range(LAYERS):
                sp.dma_start(l0w[:, l, 0:D], g0w1[l]).then_inc(l0w_in, 16)
                sp.dma_start(l0w[:, l, D:2 * D], g0w2[l]).then_inc(l0w_in, 16)
                sp.dma_start(l0w[:, l, 2 * D:3 * D], g0b2[l].partition_broadcast(P)).then_inc(l0w_in, 16)
                sp.dma_start(l0w[:, l, 3 * D:3 * D + 1], g0b1[l].unsqueeze(1)).then_inc(l0w_in, 16)
                sp.dma_start(l0w[:, l, 3 * D + 1:3 * D + 2], g0b2[l].unsqueeze(1)).then_inc(l0w_in, 16)
            sp.dma_start(tab[:, 0:R1 * D].rearrange("p (r o) -> p r o", r=R1), g1w.rearrange("r d o -> d r o")).then_inc(tab_in, 16)
            sp.dma_start(tab[:, R1 * D:(R1 + 1) * D], g1root).then_inc(tab_in, 16)
            AW = 2 * D
            for o, a in ((rows[:, 0, :], g1bias.partition_broadcast(P)),
                         (rows[:, 1, :], g2ab1.partition_broadcast(P)),
                         (rows[:, 2, :], g2aw2.rearrange("o a -> (o a)").partition_broadcast(P)),
                         (b2att[:, :], g2ab2.partition_broadcast(P)),
                         (wattn[:, 0, :], g2aw1[0:D]),
                         (wattn[:, 1, :], g2aw1[D:AW]),
                         (wattn[0:HALF, 2, :], g2aw1[AW:AW + HALF]),
                         (feT[0:DE, :], ea1[0:F].rearrange("e a -> a e")),
                         (feT[DE:HALF, :], ea2[0:F].rearrange("e a -> a e")),
                         (fidx[:, 0:1], src[0:F].rearrange("(e a) -> e a", a=1)),
                         (fidx[:, 1:2], dst[0:F].rearrange("(e a) -> e a", a=1)),
                         (basis, g2w.rearrange("b d o -> d b o")),
                         (compb[:, :, :], g2comp.partition_broadcast(P)),
                         (b3row[:, :, :], g3bias.partition_broadcast(P)),
                         (gwrow[:, :, :], g3gw.rearrange("r o a -> r (o a)").partition_broadcast(P)),
                         (gbrow[:, :], g3gb.rearrange("r a -> (r a)").partition_broadcast(P))):
                sp.dma_start(o, a).then_inc(small_in, 16)
            with sp.Fori(0, LAYERS) as l:
                for c in range(CH):
                    sp.wait_ge(un_ready, l * CH + c + 1)
                    sp.dma_start(table0[c * KB:c * KB + chunk(c)].rearrange("(b p) f -> p b f", p=P),
                                 un[:, 4 * c:4 * c + chunk(c) // P, :]).then_inc(table0_set, 16)
            sp.wait_ge(table0_set, 16 * (2 + CH * LAYERS))

            def write_table(ph, table, width):
                rows_of = table.rearrange("(n r) w -> n (r w)", n=NP)

                def body(i):
                    for q in range(QB):
                        s = q % SLOTS
                        for j in ROW_JOBS[ph]:
                            hold(sp, bank_free[bank_of(ph, q, j)], bank_use(ph, i, q, j) + 2)
                        if PARTS[ph]:
                            hold(sp, stage_ready[s], slot_parts(ph, i, q))
                        sp.dma_start(rows_of[bass.ds((i * QB + q) * P, P), :], stage[:, s, 0:width]).then_inc(stage_out[s], 16)
                nodes(sp, ph, body)

            write_table(1, table1, R1 * D)
            sp.wait_ge(tp_full, BLOCKS)
            for b in range(BANKS):
                sp.wait_ge(bank_full[b], NI * JOBS[1])
            sp.dma_start(tab[:, R2 * D:(R2 + 1) * D], g2upd).then_inc(tab_in, 16)
            write_table(2, table2, R2 * D)
            sp.wait_ge(xn_ready, 2 * BLOCKS)
            sp.dma_start(table0.rearrange("(b p) f -> p b f", p=P), xn[:, :, :]).then_inc(table0_set, 16)
            for b in range(BANKS):
                sp.wait_ge(bank_full[b], NI * (JOBS[1] + JOBS[2]))
            sp.dma_start(tab[:, 0:R3 * D].rearrange("p (r o) -> p r o", r=R3), g3w.rearrange("r d o -> d r o")).then_inc(tab_in, 16)
            sp.dma_start(tab[:, R3 * D:(R3 + 1) * D], g3loop).then_inc(tab_in, 16)
            write_table(3, table3, R3 * D)
            for s in range(SLOTS):
                sp.wait_ge(stage_out[s], 3 * NI * USES[s] * 16)
            sp.wait_ge(xn_ready, 4 * BLOCKS)
            sp.dma_start(out[0:(BLOCKS - 1) * P].rearrange("(b p) f -> p b f", p=P), xn[:, 0:BLOCKS - 1, :]).then_inc(out_done, 16)
            sp.dma_start(out[(BLOCKS - 1) * P:N], xn[0:LASTN, BLOCKS - 1, :]).then_inc(out_done, 16)
            sp.wait_ge(out_done, 32)

        @block.gpsimd
        def _(pool):
            o = 0
            for w, pat, cm in ((STEPS, [[1, STEPS]], 0), (P, [[1, P]], 0), (R2, [[1, R2]], 0), (TC, [[TQ, TC]], 1)):
                nc.gpsimd.iota(iota_i[:, o:o + w], pattern=pat, base=0, channel_multiplier=cm).then_inc(iota_set, 1)
                o += w
            nc.gpsimd.memset(ident[:, :], 0.0).then_inc(iota_set, 1)
            pool.wait_ge(iota_set, 5)
            nc.gpsimd.affine_select(out=ident[:, :], in_=ident[:, :], compare_op=ALU.not_equal, fill=1.0,
                                    base=0, pattern=[[-1, P]], channel_multiplier=1).then_inc(iota_set, 1)

            def gather_group(q, grp, base, table, idx, width):
                pool.wait_ge(group_free, base + grp + 1)
                nc.gpsimd.tensor_copy(gidx[:, q, :], idx[:, bass.ds(grp * G, G)]).then_inc(gidx_set, 1)
                pool.wait_ge(gidx_set, base + grp + 1)
                pool.nop(nofuse=True)
                for j in range(G):
                    pool.indirect_dma_start(msgs[:, q, j, 0:width], None, table,
                                            bass.IndirectOffsetOnAxis(ap=gidx[:, q, j:j + 1], axis=0)
                                            ).then_inc(msgs_in[q], 16)

            def gather_pass(base, table, idx, width):
                with pool.Fori(0, IT) as k:
                    for q in range(NB):
                        gather_group(q, k * NB + q, base, table, idx, width)

            def keep_features(ph):
                def body(i):
                    for q in range(QB):
                        hold(pool, xb_ready, seen(ph, i, q) + 1)
                        nc.gpsimd.tensor_copy(xn[:, bass.ds(i * QB + q, 1), :], xb[:, q:q + 1, :]).then_inc(xn_ready, 1)
                    if ph == 3:
                        for q in range(QB):
                            s = q % SLOTS
                            for j in (1, 2):
                                hold(pool, bank_free[bank_of(ph, q, j)], bank_use(ph, i, q, j) + 2)
                            hold(pool, gate_ready, i * QB + q + 1)
                            rows3 = stage[:, s, 0:R3 * D].rearrange("p (r w) -> p r w", r=R3)
                            nc.gpsimd.tensor_tensor(rows3, rows3, gate[:, q, :].unsqueeze(2).to_broadcast([P, R3, D]),
                                                    ALU.mult).then_inc(stage_ready[s], 1)
                nodes(pool, ph, body)

            def table_written(ph):
                for s in range(SLOTS):
                    pool.wait_ge(stage_out[s], ph * NI * USES[s] * 16)

            pool.wait_ge(walk_set, 1)
            with pool.Fori(0, LAYERS) as l:
                pool.wait_ge(table0_set, l * (16 * CH) + 32)
                pool.nop(nofuse=True)
                with pool.Fori(0, IT) as k:
                    for q in range(NB):
                        gather_group(q, k * NB + q, l * GROUPS, table0, idx0, D)
            keep_features(1)
            table_written(1)
            gather_pass(4 * GROUPS, table1, idx8, D)
            keep_features(2)
            pool.wait_ge(table0_set, 16 * (3 + CH * LAYERS))
            pool.wait_ge(small_in, SMALL * 16)
            for n in range(2):
                pool.indirect_dma_start(xe[:, n, :], None, table0,
                                        bass.IndirectOffsetOnAxis(ap=fidx[:, n:n + 1], axis=0)).then_inc(xe_in, 16)
            table_written(2)
            gather_pass(5 * GROUPS, table2, idx16, D)
            keep_features(3)
            table_written(3)
            gather_pass(6 * GROUPS, table3, idx8, D)
            keep_features(4)

        @block.tensor
        def _(pe):
            pe.sem_inc(group_free, NB)
            for s, v in [(hotT_ready, 1), (w_read, 1), (xTb_ready, 2)] + [(b, 1) for b in bank_free]:
                pe.sem_inc(s, v)
            pe.wait_ge(sel_ready, 1)
            for c in range(TC):
                last = nc.tensor.matmul(acc[:, 0:STEPS], ones[0:TQ, :], cmp_m[:, c, :], start=(c == 0), stop=(c == TC - 1))
            last.then_inc(walk_ps, 1)
            pe.wait_ge(sel_ready, 2)
            for k in range(4):
                for c in range(TC):
                    last = nc.tensor.matmul(acc[:, (k + 1) * KB:(k + 1) * KB + STEPS], ids_f[:, k, c, :], sel_m[:, c, :],
                                            start=(c == 0), stop=(c == TC - 1))
                last.then_inc(walk_ps, 1)
            pe.wait_ge(x_in, 32)
            pe.wait_ge(walk_set, 1)
            for b in range(BLOCKS):
                last = nc.tensor.transpose(acc[:, b * P:(b + 1) * P], xn[:, b, :], ident[:, :])
            last.then_inc(xT_ps, 1)

            def load_blocks(k):
                _, vals = nc.values_load_multi_w_load_instructions(
                    walk_i[0:1, 0, bass.ds(k * (G * NB), G * NB)], engines=[mybir.EngineType.PE],
                    min_val=0, max_val=(BLOCKS - 1) * P,
                    skip_runtime_bounds_check_because="a block number times 128, from the walk")
                return vals

            def clear_sums():
                for c in range(7):
                    nc.tensor.matmul(acc[:, c * KB:(c + 1) * KB], zerob[:, 0:P], zerob[:, :], start=True, stop=True)

            with pe.Fori(0, LAYERS) as l:
                pe.wait_ge(xT_ready, l * CH + 1)
                clear_sums()
                nc.tensor.matmul(misc[:, :], zerob[:, 0:P], zerob[:, :], start=True, stop=True)
                with pe.Fori(0, IT) as k:
                    blk = load_blocks(k)
                    for q in range(NB):
                        pe.wait_ge(msgs_in[q], (l * IT + k + 1) * (16 * G))
                        pe.wait_ge(hot_ready, l * GROUPS + k * NB + q + 1)
                        for j in range(G):
                            nc.tensor.matmul(cps[:, bass.ds(blk[q * G + j] // (P // R1), R1)], hot[:, q, j, :], relhot[:, q, j, :],
                                             start=False, stop=True, skip_group_check=True)
                            last = nc.tensor.matmul(acc[:, bass.ds(blk[q * G + j], P)], msgs[:, q, j, 0:D], hot[:, q, j, :],
                                                    start=False, stop=True, skip_group_check=True)
                        last.then_inc(group_free, 1)

                def second(c):
                    pe.wait_ge(rT_ready, l * CH + c + 1)
                    nc.tensor.matmul(acc[:, c * KB:c * KB + chunk(c)], l0c[:, D:2 * D], rT[:, c * KB:c * KB + chunk(c)],
                                     start=True, stop=True).then_inc(xT_ps, 1)
                    if c:
                        pe.wait_ge(un_ready, l * CH + c)
                    for b in range(chunk(c) // P):
                        last = nc.tensor.matmul(misc[:, b * P:(b + 1) * P], rT[:, c * KB + b * P:c * KB + (b + 1) * P],
                                                l0c[:, D:2 * D], start=True, stop=True)
                    last.then_inc(un_ps, 1)

                for c in range(CH):
                    pe.wait_ge(hT_ready, l * CH + c + 1)
                    nc.tensor.matmul(acc[:, c * KB:c * KB + chunk(c)], l0c[:, 0:D], hT[:, c * KB:c * KB + chunk(c)],
                                     start=True, stop=True).then_inc(m1_ps, 1)
                    if c:
                        second(c - 1)
                second(CH - 1)
                hold(pe, un_ready, l * CH + CH)

            def node_products(ph):
                def body(i):
                    def tp(q):
                        pe.wait_ge(xb_ready, seen(ph, i, q) + 1)
                        pe.wait_ge(xTb_ready, seen(ph, i, q) + 1)
                        o = (5 + q % 2) * KB
                        nc.tensor.transpose(acc[:, o:o + P], xb[:, q, :], ident[:, :]).then_inc(tp_full, 1)
                    tp(0)
                    for q in range(QB):
                        if q + 1 < QB:
                            tp(q + 1)
                        pe.wait_ge(xTb_ready, seen(ph, i, q) + 3)
                        for j, (c0, c1) in enumerate(products(ph)):
                            b = bank_of(ph, q, j)
                            pe.wait_ge(bank_free[b], bank_use(ph, i, q, j) + 1)
                            nc.tensor.matmul(acc[:, b * KB:b * KB + c1 - c0], xTb[:, q, :], tab[:, c0:c1],
                                             start=True, stop=True).then_inc(bank_full[b], 1)
                pe.wait_ge(tab_set, ph)
                nodes(pe, ph, body)
                pe.wait_ge(xTb_ready, ph * BLOCKS + 2)
                for b in range(BANKS):
                    pe.wait_ge(bank_free[b], NI * sum(JOBS[p] for p in range(1, ph + 1)) + 1)
                clear_sums()

            def add_up(q, k, base, blk):
                pe.wait_ge(msgs_in[q], k * (16 * G) + (base // GROUPS * IT + 1) * (16 * G))
                pe.wait_ge(hot_ready, k * NB + (base + q + 1))
                for j in range(G):
                    last = nc.tensor.matmul(acc[:, bass.ds(blk[q * G + j], P)], hot[:, q, j, :], msgs[:, q, j, 0:D],
                                            start=False, stop=True, skip_group_check=True)
                last.then_inc(group_free, 1)

            node_products(1)
            with pe.Fori(0, IT) as k:
                blk = load_blocks(k)

                def transposes(q):
                    g = k * NB + q
                    pe.wait_ge(hotb_ready, g + 1)
                    pe.wait_ge(w_read, g + 1)
                    for j in range(G):
                        last = nc.tensor.transpose(hotT_ps[:, j, :], hotb[:, q, j, :], identb[:, :])
                    last.then_inc(hotT_ps_full, 1)

                def weights(q):
                    g = k * NB + q
                    pe.wait_ge(hotT_ready, g + 2)
                    for j in range(G):
                        last = nc.tensor.matmul(wps[:, j, :], hotT[:, q, j, :],
                                                invc[:, bass.ds(blk[q * G + j] // (P // R1), R1)], start=True, stop=True)
                    last.then_inc(w_ps_full, 1)
                for q in range(NB):
                    transposes(q)
                    if q:
                        add_up(q - 1, k, 4 * GROUPS, blk)
                    weights(q)
                add_up(NB - 1, k, 4 * GROUPS, blk)

            node_products(2)
            pe.wait_ge(xe_in, 32)
            for n in range(2):
                last = nc.tensor.transpose(misc[:, n * F:(n + 1) * F], xe[:, n, :], ident[0:F, 0:F])
            last.then_inc(xeT_ps, 1)
            pe.wait_ge(xeT_ready, 1)
            nc.tensor.matmul(misc[0:F, 0:D], xeT[:, 0:F], wattn[:, 0, :], start=True, stop=False)
            nc.tensor.matmul(misc[0:F, 0:D], xeT[:, F:2 * F], wattn[:, 1, :], start=False, stop=False)
            nc.tensor.matmul(misc[0:F, 0:D], feT[:, :], wattn[0:HALF, 2, :], start=False, stop=True).then_inc(h_ps_full, 1)
            pe.wait_ge(alpha_ready, 2)
            nc.tensor.matmul(misc[:, 0:F], alphab[:, :], ident[0:F, 0:F], start=True, stop=True).then_inc(h_ps_full, 1)
            with pe.Fori(0, IT) as k:
                blk = load_blocks(k)
                for q in range(NB):
                    add_up(q, k, 5 * GROUPS, blk)

            node_products(3)
            with pe.Fori(0, IT) as k:
                blk = load_blocks(k)
                for q in range(NB):
                    add_up(q, k, 6 * GROUPS, blk)

        @block.scalar
        def _(act):
            act.wait_ge(xT_ps, 1)
            for c in range(CH):
                last = nc.scalar.activation(xT[:, c * KB:c * KB + chunk(c)], acc[:, c * KB:c * KB + chunk(c)], ACT.Copy)
            last.then_inc(xT_ready, 1)
            with act.Fori(0, LAYERS) as l:
                act.wait_ge(l0c_set, l + 1)

                def relu_part(c):
                    act.wait_ge(m1_ps, l * CH + c + 1)
                    nc.scalar.activation(rT[:, c * KB:c * KB + chunk(c)], acc[:, c * KB:c * KB + chunk(c)], ACT.Relu,
                                         bias=l0c[:, 3 * D:3 * D + 1]).then_inc(rT_ready, 1)

                def xT_part(c):
                    act.wait_ge(xT_ps, l * CH + c + 2)
                    nc.scalar.activation(xT[:, c * KB:c * KB + chunk(c)], acc[:, c * KB:c * KB + chunk(c)], ACT.Identity,
                                         bias=l0c[:, 3 * D + 1:3 * D + 2]).then_inc(xT_ready, 1)
                for c in range(CH):
                    relu_part(c)
                    if c:
                        xT_part(c - 1)
                xT_part(CH - 1)

            def node_copies(ph):
                def body(i):
                    act.wait_ge(bag_ready, i + ((ph - 1) * NI + 1))
                    nc.scalar.activation(std[:, :], bag[:, :, 1], ACT.Sqrt, bias=epst[:, :]).then_inc(std_ready, 1)
                    if ph == 4:
                        return

                    def tp(q):
                        act.wait_ge(tp_full, seen(ph, i, q) + 1)
                        for j in range(JOBS[ph]):
                            b = bank_of(ph, q, j)
                            after(act, bank_full[b], bank_use(ph, i, q, j) - JOBS[ph] + 1 if ph > 1 or not isinstance(i, int) else 0)
                        o = (5 + q % 2) * KB
                        nc.scalar.activation(xTb[:, q, :], acc[:, o:o + P], ACT.Copy).then_inc(xTb_ready, 1)
                    tp(0)
                    for q in range(QB):
                        if q + 1 < QB:
                            tp(q + 1)
                        s = q % SLOTS
                        if ph == 1:
                            parts = [(0, stage[:, s, 0:KB])]
                        elif ph == 2:
                            parts = [(j, stage[:, s, j * KB:(j + 1) * KB]) for j in (0, 2)]
                        else:
                            parts = []
                            act.wait_ge(glog_ready, i * QB + q + 1)
                            nc.scalar.activation(gate[:, q, :], glog[:, q, :], ACT.Sigmoid).then_inc(gate_ready, 1)
                        for n, (j, o) in enumerate(parts):
                            b = bank_of(ph, q, j)
                            if n == 0:
                                after(act, stage_out[s], slot_use(ph, i, q) * 16)
                            act.wait_ge(bank_full[b], bank_use(ph, i, q, j) + 1)
                            nc.scalar.activation(o, acc[:, b * KB:(b + 1) * KB], ACT.Copy).then_inc(bank_free[b], 1)
                nodes(act, ph, body)

            node_copies(1)
            with act.Fori(0, IT) as k:
                for q in range(NB):
                    act.wait_ge(hotT_ps_full, k * NB + (q + 1))
                    act.wait_ge(group_free, k * NB + (4 * GROUPS + q + 1))
                    nc.scalar.activation(hotT[:, q, :, :], hotT_ps, ACT.Copy).then_inc(hotT_ready, 1)
            node_copies(2)
            act.wait_ge(xeT_ps, 1)
            nc.scalar.activation(xeT[:, :], misc[:, 0:2 * F], ACT.Copy).then_inc(xeT_ready, 1)
            act.wait_ge(logit_ready, 1)
            nc.scalar.activation(alpha[:, :], logit[:, :], ACT.Sigmoid, bias=b2att[0:F, :]).then_inc(alpha_ready, 1)
            node_copies(3)
            node_copies(4)

        @block.vector
        def _(dve):
            n = [0]

            def link(ins):
                n[0] += 1
                ins.then_inc(setup_dve, 1)
                dve.wait_ge(setup_dve, n[0])

            nc.vector.memset(ids_i[:, 0, TC - 1, :], -1).then_inc(pads_set, 1)
            nc.vector.memset(ids_i[:, 1:4, TC - 1, :], 0).then_inc(pads_set, 1)
            nc.vector.memset(xn[:, BLOCKS - 1, :], 0.0).then_inc(pads_set, 1)
            nc.vector.memset(ones[:, :], 1.0)
            nc.vector.memset(epst[:, :], EPS)
            nc.vector.memset(zerob[:, :], 0.0).then_inc(pads_set, 1)
            dve.wait_ge(iota_set, 6)
            o = 0
            for t, w in ((step_io, STEPS), (node_io, P), (rel_io, R2), (tile_io, TC)):
                link(nc.vector.tensor_copy(t[:, :], iota_i[:, o:o + w]))
                o += w
            link(nc.vector.tensor_copy(identb[:, :], ident[:, :]))
            dve.wait_ge(ids_in, 12 * 16)
            link(nc.vector.tensor_copy(ids_f, ids_i))
            link(nc.vector.tensor_reduce(tmax[0:TQ, 0, :], ids_f[:, 0, :, :], AXX, ALU.max))
            link(nc.vector.tensor_copy(tmax_i[0:TQ, 0, :], tmax[0:TQ, 0, :]))
            link(nc.vector.tensor_single_scalar(tmax_i[0:TQ, 1, :], tmax_i[0:TQ, 0, :], 7, ALU.arith_shift_right))
            link(nc.vector.tensor_copy(tmax[0:TQ, 1, :], tmax_i[0:TQ, 1, :]))
            link(nc.vector.tensor_tensor(tmax[0:TQ, 2, :], tmax[0:TQ, 1, :], tile_io[0:TQ, :], ALU.add))
            link(nc.vector.tensor_scalar(tmax[0:TQ, 3, :], tile_io[0:TQ, :], float(TILES - 1), 1e6, ALU.is_ge, ALU.mult))
            link(nc.vector.tensor_tensor(tmax[0:TQ, 2, :], tmax[0:TQ, 2, :], tmax[0:TQ, 3, :], ALU.max))
            for c in range(TC):
                last = nc.vector.tensor_scalar(cmp_m[:, c, :], step_io[0:TQ, :], tmax[0:TQ, 2, c:c + 1], None, ALU.is_gt)
            last.then_inc(sel_ready, 1)
            dve.wait_ge(walk_ps, 1)
            link(nc.vector.tensor_copy(ts_f[:, :], acc[:, 0:STEPS]))
            link(nc.vector.tensor_tensor(bs_f[:, :], step_io[:, :], ts_f[:, :], ALU.subtract))
            for c in range(TC):
                last = nc.vector.tensor_scalar(sel_m[:, c, :], ts_f[0:TQ, :], tile_io[0:TQ, c:c + 1], None, ALU.is_equal)
            last.then_inc(sel_ready, 1)
            nc.vector.tensor_scalar(walk_i[0:1, 0, :], bs_f[0:1, :], float(P), None, ALU.mult)
            nc.vector.tensor_scalar(walk_i[0:1, 2, :], ts_f[0:1, :], float(P), None, ALU.mult)
            dve.wait_ge(walk_ps, 5)
            sel = [acc[:, (k + 1) * KB:(k + 1) * KB + STEPS] for k in range(4)]
            nc.vector.scalar_tensor_tensor(drel[:, :], bs_f[:, :], -float(P), sel[0], ALU.mult, ALU.add)
            nc.vector.tensor_copy(rel8[:, :], sel[2])
            nc.vector.tensor_copy(rel16[:, :], sel[3])
            nc.vector.tensor_copy(idx0[:, :], sel[1])
            link(nc.vector.tensor_copy(srcs[:, :], sel[1]))
            nc.vector.scalar_tensor_tensor(idx8[:, :], srcs[:, :], float(R1), sel[2], ALU.mult, ALU.add)
            nc.vector.scalar_tensor_tensor(idx16[:, :], srcs[:, :], float(R2), sel[3], ALU.mult, ALU.add).then_inc(walk_set, 1)
            dve.wait_ge(walk_set, 1)
            dve.wait_ge(l0w_in, LAYERS * 5 * 16)

            def one_hot(o, s):
                return nc.vector.tensor_tensor(
                    o, node_io[:, :].unsqueeze(1).to_broadcast([P, G, P]),
                    drel[:, bass.ds(s, G)].unsqueeze(2).to_broadcast([P, G, P]), ALU.is_equal)

            def one_hot_rel(q, s):
                return nc.vector.tensor_tensor(
                    relhot[:, q, :, :], rel_io[:, 0:R1].unsqueeze(1).to_broadcast([P, G, R1]),
                    rel8[:, bass.ds(s, G)].unsqueeze(2).to_broadcast([P, G, R1]), ALU.is_equal)

            with dve.Fori(0, LAYERS) as l:
                dve.wait_ge(xT_ready, l * CH + 1)
                nc.vector.tensor_copy(l0c[:, :], l0w[:, bass.ds(l, 1), :]).then_inc(l0c_set, 1)
                with dve.Fori(0, IT) as k:
                    for q in range(NB):
                        dve.wait_ge(group_free, l * GROUPS + k * NB + q + 1)
                        one_hot_rel(q, k * (G * NB) + q * G)
                        one_hot(hot[:, q, :, :], k * (G * NB) + q * G).then_inc(hot_ready, 1)
                dve.wait_ge(group_free, l * GROUPS + (GROUPS + NB))
                nc.vector.tensor_copy(cnt[:, :, :], cps.rearrange("p (b r) -> p b r", r=R1))
                for c in range(CH):
                    nc.vector.tensor_tensor(hT[:, c * KB:c * KB + chunk(c)], acc[:, c * KB:c * KB + chunk(c)],
                                            xT[:, c * KB:c * KB + chunk(c)], ALU.add).then_inc(hT_ready, 1)
                for c in range(CH):
                    dve.wait_ge(un_ps, l * CH + c + 1)
                    nb = chunk(c) // P
                    nc.vector.tensor_tensor(un[:, 4 * c:4 * c + nb, :], misc[:, 0:chunk(c)].rearrange("p (b f) -> p b f", f=D),
                                            l0c[:, 2 * D:3 * D].unsqueeze(1).to_broadcast([P, nb, D]), ALU.add
                                            ).then_inc(un_ready, 1)
                dve.wait_ge(un_ready, l * CH + CH)
                dve.nop(nofuse=True)

            dve.wait_ge(small_in, SMALL * 16)
            link(nc.vector.tensor_scalar(invc[:, :], cnt[:, :, :].rearrange("p b r -> p (b r)"), 1.0, None, ALU.max))
            link(nc.vector.reciprocal(invc[:, :], invc[:, :]))
            link(nc.vector.tensor_reduce(indeg[:, :], cnt[:, :, :], AXX, ALU.add))

            steps = {"chain": 0}

            def hop(ins, per, at_):
                ins.then_inc(chain, 1)
                hold(dve, chain, per + (at_ + steps["chain"]))

            def node_norm(ph):
                CPI = 4

                def body(i):
                    if ph > 1 or not isinstance(i, int):
                        dve.wait_ge(xn_ready, seen(ph, i))
                        if ph < 4:
                            dve.wait_ge(tp_full, seen(ph, i))
                    blocks = bass.ds(i * QB, QB)
                    if ph == 1:
                        ins = nc.vector.tensor_tensor(yb[:, :, :], un[:, blocks, :], xn[:, blocks, :], ALU.add)
                    else:
                        ins = nc.vector.scalar_tensor_tensor(yb[:, :, :].rearrange("p b f -> p (b f)"),
                                                             un[:, blocks, :].rearrange("p b f -> p (b f)"), 0.0,
                                                             xn[:, blocks, :].rearrange("p b f -> p (b f)"), ALU.max, ALU.add)
                    hop(ins, i * CPI, 1)
                    for q in range(QB):
                        ins = nc.vector.bn_stats(bst[:, q, :], yb[:, q, :])
                    hop(ins, i * CPI, 2)
                    for q in range(QB):
                        ins = nc.vector.bn_aggr(bag[:, q, :], bst[:, q, :])
                    ins.then_inc(bag_ready, 1)
                    dve.wait_ge(std_ready, i + ((ph - 1) * NI + 1))
                    hop(nc.vector.reciprocal(rstd[:, :], std[:, :]), i * CPI, 3)
                    for q in range(QB):
                        nc.vector.tensor_scalar(xb[:, q, :], yb[:, q, :], bag[:, q, 0:1], rstd[:, q:q + 1],
                                                ALU.subtract, ALU.mult).then_inc(xb_ready, 1)
                    dve.wait_ge(xb_ready, seen(ph, i) + QB)
                    dve.nop(nofuse=True)
                    nc.vector.engine_nop().then_inc(chain, 1)
                    if ph == 4:
                        return
                    for q in range(QB):
                        s = q % SLOTS
                        bk = [acc[:, bank_of(ph, q, j) * KB:(bank_of(ph, q, j) + 1) * KB] for j in range(JOBS[ph])]

                        def full(j):
                            dve.wait_ge(bank_full[bank_of(ph, q, j)], bank_use(ph, i, q, j) + 1)

                        def freed(ins, j):
                            ins.then_inc(bank_free[bank_of(ph, q, j)], 1)
                        b1 = bass.ds(i * QB + q, 1)
                        if ph == 1:
                            after(dve, stage_out[s], slot_use(ph, i, q) * 16)
                            full(1)
                            freed(nc.vector.tensor_copy(stage[:, s, KB:2 * KB], bk[1]), 1)
                            full(2)
                            freed(nc.vector.tensor_tensor(rest[:, b1, :].rearrange("p b f -> p (b f)"), bk[2][:, 0:D], rows[:, 0, :], ALU.add), 2)
                        elif ph == 2:
                            dve.wait_ge(stage_out[s], slot_use(ph, i, q) * 16)
                            for j in (1, 3):
                                full(j)
                                freed(nc.vector.tensor_copy(stage[:, s, j * KB:(j + 1) * KB], bk[j]), j)
                            full(4)
                            freed(nc.vector.tensor_scalar(rest[:, b1, :].rearrange("p b f -> p (b f)"), bk[4][:, 0:D],
                                                          indeg[:, bass.ds(i * QB + q, 1)], None, ALU.mult), 4)
                        else:
                            dve.wait_ge(stage_out[s], slot_use(ph, i, q) * 16)
                            full(0)
                            nc.vector.tensor_tensor(glog[:, q, :], bk[0][:, D:D + R3], gcon[:, :], ALU.add).then_inc(glog_ready, 1)
                            freed(nc.vector.tensor_copy(rest[:, b1, :].rearrange("p b f -> p (b f)"), bk[0][:, 0:D]), 0)
                            for j in (1, 2):
                                full(j)
                                ins = nc.vector.tensor_tensor(stage[:, s, (j - 1) * KB:j * KB], bk[j],
                                                              b3row[:, :, :].rearrange("p r o -> p (r o)")[:, (j - 1) * KB:j * KB], ALU.add)
                                freed(ins, j)
                nodes(dve, ph, body)
                steps["chain"] += CPI * NI

            def read_sums(base):
                dve.wait_ge(group_free, base + GROUPS + NB)
                for c in range(CH):
                    nb = chunk(c) // P
                    last = nc.vector.tensor_tensor(un[:, 4 * c:4 * c + nb, :].rearrange("p b f -> p (b f)"),
                                                   acc[:, c * KB:c * KB + chunk(c)],
                                                   rest[:, 4 * c:4 * c + nb, :].rearrange("p b f -> p (b f)"), ALU.add)
                link(last)

            dve.wait_ge(tab_in, 32)
            nc.vector.engine_nop().then_inc(tab_set, 1)
            node_norm(1)
            dve.wait_ge(tab_in, 3 * 16)
            for r in range(R2):
                o = tab[:, r * D:(r + 1) * D]
                for b in range(BASES):
                    if b == 0:
                        ins = nc.vector.tensor_scalar(o, basis[:, 0, :], compb[:, r, 0:1], None, ALU.mult)
                    else:
                        ins = nc.vector.scalar_tensor_tensor(o, basis[:, b, :], compb[:, r, b:b + 1], o, ALU.mult, ALU.add)
                    link(ins)
            nc.vector.engine_nop().then_inc(tab_set, 1)
            with dve.Fori(0, IT) as k:
                def plain1(q):
                    dve.wait_ge(group_free, k * NB + (4 * GROUPS + q + 1))
                    one_hot_rel(q, k * (G * NB) + q * G)
                    one_hot(hotb[:, q, :, :], k * (G * NB) + q * G).then_inc(hotb_ready, 1)
                plain1(0)
                plain1(1)
                for q in range(NB):
                    dve.wait_ge(w_ps_full, k * NB + (q + 1))
                    hop(nc.vector.tensor_tensor(wsum[:, :, :], wps, relhot[:, q, :, :], ALU.mult), k * (2 * NB), 2 * q + 1)
                    dve.sem_inc(w_read, 1)
                    hop(nc.vector.tensor_reduce(wedge[:, q, :], wsum[:, :, :], AXX, ALU.add), k * (2 * NB), 2 * q + 2)
                    nc.vector.tensor_tensor(hot[:, q, :, :], hotb[:, q, :, :],
                                            wedge[:, q, :].unsqueeze(2).to_broadcast([P, G, P]), ALU.mult).then_inc(hot_ready, 1)
                    if q + 2 < NB:
                        plain1(q + 2)
            steps["chain"] += 2 * NB * IT
            read_sums(4 * GROUPS)
            node_norm(2)
            dve.wait_ge(tab_in, 5 * 16)
            gtmp = un[:, 0:R3, :]
            link(nc.vector.tensor_tensor(gtmp, tab[:, 0:R3 * D].rearrange("p (r o) -> p r o", r=R3), gwrow[:, :, :], ALU.mult))
            link(nc.vector.tensor_reduce(tab[:, (R3 + 1) * D:(R3 + 1) * D + R3], gtmp, AXX, ALU.add))
            link(nc.vector.tensor_tensor(gtmp, b3row[:, :, :], gwrow[:, :, :], ALU.mult))
            link(nc.vector.tensor_reduce(gcon[:, :], gtmp, AXX, ALU.add))
            link(nc.vector.tensor_tensor(gcon[:, :], gcon[:, :], gbrow[:, :], ALU.add))
            nc.vector.engine_nop().then_inc(tab_set, 1)
            dve.wait_ge(h_ps_full, 1)
            link(nc.vector.tensor_tensor(hsum[:, :], misc[0:F, 0:D], rows[0:F, 1, :], ALU.add))
            nc.vector.scalar_tensor_tensor(hdot[:, :], hsum[:, :], 0.0, rows[0:F, 2, :], ALU.max, ALU.mult,
                                           accum_out=logit[:, :]).then_inc(logit_ready, 1)
            dve.wait_ge(alpha_ready, 1)
            nc.vector.tensor_scalar(alphab[:, :], ones[0:F, :], alpha[:, :], None, ALU.mult).then_inc(alpha_ready, 1)
            dve.wait_ge(h_ps_full, 2)
            link(nc.vector.tensor_copy(alphar[:, :], misc[:, 0:F]))
            with dve.Fori(0, IT) as k:
                for q in range(NB):
                    s0 = k * (G * NB) + q * G
                    dve.wait_ge(group_free, k * NB + (5 * GROUPS + q + 1))
                    one_hot(hotb[:, q, :, :], s0)
                    hop(nc.vector.tensor_tensor(relhot2[:, :, :], rel_io[:, :].unsqueeze(1).to_broadcast([P, G, R2]),
                                                rel16[:, bass.ds(s0, G)].unsqueeze(2).to_broadcast([P, G, R2]), ALU.is_equal),
                        k * (3 * NB), 3 * q + 1)
                    hop(nc.vector.tensor_tensor(wsum2[:, :, :], relhot2[:, :, :], alphar[:, :].unsqueeze(1).to_broadcast([P, G, R2]),
                                                ALU.mult), k * (3 * NB), 3 * q + 2)
                    hop(nc.vector.tensor_reduce(wedge[:, q, :], wsum2[:, :, :], AXX, ALU.add), k * (3 * NB), 3 * q + 3)
                    nc.vector.tensor_tensor(hot[:, q, :, :], hotb[:, q, :, :],
                                            wedge[:, q, :].unsqueeze(2).to_broadcast([P, G, P]), ALU.mult).then_inc(hot_ready, 1)
            steps["chain"] += 3 * NB * IT
            read_sums(5 * GROUPS)
            node_norm(3)
            with dve.Fori(0, IT) as k:
                for q in range(NB):
                    dve.wait_ge(group_free, k * NB + (6 * GROUPS + q + 1))
                    one_hot(hot[:, q, :, :], k * (G * NB) + q * G).then_inc(hot_ready, 1)
            read_sums(6 * GROUPS)
            node_norm(4)


_INS = ['x', 'src', 'dst', 'edge_attr_32', 'edge_attr_32_n2', 'edge_type_16', 'edge_type_8',
        'L0_gnn_W1', 'L0_gnn_b1', 'L0_gnn_W2', 'L0_gnn_b2', 'L1_gnn_W', 'L1_gnn_root', 'L1_gnn_bias',
        'L2_gnn_weight', 'L2_gnn_comp', 'L2_gnn_attn_w1', 'L2_gnn_attn_b1', 'L2_gnn_attn_w2', 'L2_gnn_attn_b2',
        'L2_gnn_update', 'L3_gnn_W', 'L3_gnn_bias_term', 'L3_gnn_gate_weight', 'L3_gnn_gate_bias', 'L3_gnn_loop_weight']
_OUTS = [((N, D), 'float32')]


def kernel(**inputs):
    import numpy as _np
    import concourse.bacc as _bacc
    from concourse import mybir as _mybir
    from concourse.bass_utils import run_bass_kernel_spmd as _run

    nc = _bacc.Bacc("TRN2", target_bir_lowering=False, num_devices=1)
    arrays, args = {}, []
    for name in _INS:
        a = _np.ascontiguousarray(inputs[name])
        arrays[f"in_{name}_dram"] = a
        args.append(nc.dram_tensor(f"in_{name}_dram", a.shape, _mybir.dt.from_np(a.dtype), kind="ExternalInput").ap())
    for i, (shape, dtype) in enumerate(_OUTS):
        dt = _mybir.dt.from_np(_np.dtype(dtype))
        args.append(nc.dram_tensor(f"out_{i}_dram", shape, dt, kind="ExternalOutput").ap())
    gnn(nc, *args)
    r = _run(nc, [arrays], core_ids=[0])
    return r.results[0]["out_0_dram"]
```
